# Optimizing a Trainium2 kernel written in Bass

```python
import numpy as np
import jax
import jax.numpy as jnp

def _softmax(x, axis=-1):
    return jax.nn.softmax(x, axis=axis)

def _gelu(x):
    return jax.nn.gelu(x, approximate=True)

def _silu(x):
    return jax.nn.silu(x)

def _sigmoid(x):
    return jax.nn.sigmoid(x)

def _layernorm(x, axis=-1, eps=1e-05):
    m = jnp.mean(x, axis=axis, keepdims=True)
    v = jnp.var(x, axis=axis, keepdims=True)
    return (x - m) / jnp.sqrt(v + eps)

def _scatter_add(tgt, idx, src, axis=0):
    return tgt.at[idx].add(src)

def _segment_sum(src, seg, n):
    return jax.ops.segment_sum(src, seg, n)
kernel_name = 'mk_dlrm_tower_d1_rec_r8_d3a3b1'

def setup_inputs(seed: int=0):
    np.random.seed(seed)
    _w = jnp.asarray

    def _rec_inputs():
        import jax
        import jax.numpy as jnp
        _tk = jax.random.key(seed)
        ids = jnp.stack([jax.random.randint(jax.random.fold_in(_tk, 200 + f), (512,), 0, v, jnp.int32) for f, v in enumerate([12500, 12500, 125000, 12500, 1000, 12500, 1000, 1250, 1250, 12500, 1250, 1000, 12500, 1000, 1250, 1250, 12500, 1000, 12500, 1250, 1000, 1250, 1250, 1250, 1250, 1000])], axis=1)
        tbl_0 = 0.05 * jax.random.normal(jax.random.fold_in(_tk, 500 + 0), (12500, 128), jnp.float32)
        tbl_1 = 0.05 * jax.random.normal(jax.random.fold_in(_tk, 500 + 1), (12500, 128), jnp.float32)
        tbl_2 = 0.05 * jax.random.normal(jax.random.fold_in(_tk, 500 + 2), (125000, 128), jnp.float32)
        tbl_3 = 0.05 * jax.random.normal(jax.random.fold_in(_tk, 500 + 3), (12500, 128), jnp.float32)
        tbl_4 = 0.05 * jax.random.normal(jax.random.fold_in(_tk, 500 + 4), (1000, 128), jnp.float32)
        tbl_5 = 0.05 * jax.random.normal(jax.random.fold_in(_tk, 500 + 5), (12500, 128), jnp.float32)
        tbl_6 = 0.05 * jax.random.normal(jax.random.fold_in(_tk, 500 + 6), (1000, 128), jnp.float32)
        tbl_7 = 0.05 * jax.random.normal(jax.random.fold_in(_tk, 500 + 7), (1250, 128), jnp.float32)
        tbl_8 = 0.05 * jax.random.normal(jax.random.fold_in(_tk, 500 + 8), (1250, 128), jnp.float32)
        tbl_9 = 0.05 * jax.random.normal(jax.random.fold_in(_tk, 500 + 9), (12500, 128), jnp.float32)
        tbl_10 = 0.05 * jax.random.normal(jax.random.fold_in(_tk, 500 + 10), (1250, 128), jnp.float32)
        tbl_11 = 0.05 * jax.random.normal(jax.random.fold_in(_tk, 500 + 11), (1000, 128), jnp.float32)
        tbl_12 = 0.05 * jax.random.normal(jax.random.fold_in(_tk, 500 + 12), (12500, 128), jnp.float32)
        tbl_13 = 0.05 * jax.random.normal(jax.random.fold_in(_tk, 500 + 13), (1000, 128), jnp.float32)
        tbl_14 = 0.05 * jax.random.normal(jax.random.fold_in(_tk, 500 + 14), (1250, 128), jnp.float32)
        tbl_15 = 0.05 * jax.random.normal(jax.random.fold_in(_tk, 500 + 15), (1250, 128), jnp.float32)
        tbl_16 = 0.05 * jax.random.normal(jax.random.fold_in(_tk, 500 + 16), (12500, 128), jnp.float32)
        tbl_17 = 0.05 * jax.random.normal(jax.random.fold_in(_tk, 500 + 17), (1000, 128), jnp.float32)
        tbl_18 = 0.05 * jax.random.normal(jax.random.fold_in(_tk, 500 + 18), (12500, 128), jnp.float32)
        tbl_19 = 0.05 * jax.random.normal(jax.random.fold_in(_tk, 500 + 19), (1250, 128), jnp.float32)
        tbl_20 = 0.05 * jax.random.normal(jax.random.fold_in(_tk, 500 + 20), (1000, 128), jnp.float32)
        tbl_21 = 0.05 * jax.random.normal(jax.random.fold_in(_tk, 500 + 21), (1250, 128), jnp.float32)
        tbl_22 = 0.05 * jax.random.normal(jax.random.fold_in(_tk, 500 + 22), (1250, 128), jnp.float32)
        tbl_23 = 0.05 * jax.random.normal(jax.random.fold_in(_tk, 500 + 23), (1250, 128), jnp.float32)
        tbl_24 = 0.05 * jax.random.normal(jax.random.fold_in(_tk, 500 + 24), (1250, 128), jnp.float32)
        tbl_25 = 0.05 * jax.random.normal(jax.random.fold_in(_tk, 500 + 25), (1000, 128), jnp.float32)
        _rk = jax.random.fold_in(_tk, 7)
        r_dense_features = -0.000292821 + 1.00034 * jax.random.normal(jax.random.fold_in(_rk, 101), (512, 128), jnp.float32)
        W_top1 = 0.0405887 * jax.random.normal(jax.random.fold_in(_tk, 801), (607, 512), jnp.float32)
        W_top2 = 0.0441942 * jax.random.normal(jax.random.fold_in(_tk, 802), (512, 256), jnp.float32)
        W_top3 = 0.0625 * jax.random.normal(jax.random.fold_in(_tk, 803), (256, 1), jnp.float32)
        b_top1 = jnp.zeros((512,), jnp.float32)
        b_top2 = jnp.zeros((256,), jnp.float32)
        return (r_dense_features, ids, tbl_0, tbl_1, tbl_2, tbl_3, tbl_4, tbl_5, tbl_6, tbl_7, tbl_8, tbl_9, tbl_10, tbl_11, tbl_12, tbl_13, tbl_14, tbl_15, tbl_16, tbl_17, tbl_18, tbl_19, tbl_20, tbl_21, tbl_22, tbl_23, tbl_24, tbl_25, W_top1, b_top1, W_top2, b_top2, W_top3)
    r_dense_features, ids, tbl_0, tbl_1, tbl_2, tbl_3, tbl_4, tbl_5, tbl_6, tbl_7, tbl_8, tbl_9, tbl_10, tbl_11, tbl_12, tbl_13, tbl_14, tbl_15, tbl_16, tbl_17, tbl_18, tbl_19, tbl_20, tbl_21, tbl_22, tbl_23, tbl_24, tbl_25, W_top1, b_top1, W_top2, b_top2, W_top3 = _rec_inputs()

    def _L0_rec_setup():
        import jax, jax.numpy as jnp
        import numpy as np
        F = 26
        _TRIU_I, _TRIU_J = np.triu_indices(F + 1, k=1)
        key = jax.random.key(seed)
        k1, k2 = jax.random.split(key)
        B, D = (4096, 128)
        dense_features = jax.random.normal(k1, (B, D), dtype=jnp.float32)
        sparse_features = jax.random.normal(k2, (B, F, D), dtype=jnp.float32)
        return {'dense_features': dense_features, 'sparse_features': sparse_features}
    _L0_rec_all = _L0_rec_setup()
    _L0_rec_in = {k: v for k, v in _L0_rec_all.items() if k in ()}
    del _L0_rec_all
    return {'r_dense_features': r_dense_features, 'ids': ids, 'tbl_0': tbl_0, 'tbl_1': tbl_1, 'tbl_2': tbl_2, 'tbl_3': tbl_3, 'tbl_4': tbl_4, 'tbl_5': tbl_5, 'tbl_6': tbl_6, 'tbl_7': tbl_7, 'tbl_8': tbl_8, 'tbl_9': tbl_9, 'tbl_10': tbl_10, 'tbl_11': tbl_11, 'tbl_12': tbl_12, 'tbl_13': tbl_13, 'tbl_14': tbl_14, 'tbl_15': tbl_15, 'tbl_16': tbl_16, 'tbl_17': tbl_17, 'tbl_18': tbl_18, 'tbl_19': tbl_19, 'tbl_20': tbl_20, 'tbl_21': tbl_21, 'tbl_22': tbl_22, 'tbl_23': tbl_23, 'tbl_24': tbl_24, 'tbl_25': tbl_25, 'W_top1': W_top1, 'b_top1': b_top1, 'W_top2': W_top2, 'b_top2': b_top2, 'W_top3': W_top3}

def reference(r_dense_features, ids, tbl_0, tbl_1, tbl_2, tbl_3, tbl_4, tbl_5, tbl_6, tbl_7, tbl_8, tbl_9, tbl_10, tbl_11, tbl_12, tbl_13, tbl_14, tbl_15, tbl_16, tbl_17, tbl_18, tbl_19, tbl_20, tbl_21, tbl_22, tbl_23, tbl_24, tbl_25, W_top1, b_top1, W_top2, b_top2, W_top3):
    import jax
    import jax.numpy as jnp

    def _L0_rec_ref(dense_features, sparse_features):
        import jax, jax.numpy as jnp
        import numpy as np
        F = 26
        _TRIU_I, _TRIU_J = np.triu_indices(F + 1, k=1)
        combined = jnp.concatenate([dense_features[:, None, :], sparse_features], axis=1)
        interactions = jnp.einsum('bfd,bgd->bfg', combined, combined)
        interactions_flat = interactions[:, _TRIU_I, _TRIU_J]
        return jnp.concatenate([dense_features, interactions_flat], axis=1)
    e = jnp.stack([tbl_0[ids[:, 0]], tbl_1[ids[:, 1]], tbl_2[ids[:, 2]], tbl_3[ids[:, 3]], tbl_4[ids[:, 4]], tbl_5[ids[:, 5]], tbl_6[ids[:, 6]], tbl_7[ids[:, 7]], tbl_8[ids[:, 8]], tbl_9[ids[:, 9]], tbl_10[ids[:, 10]], tbl_11[ids[:, 11]], tbl_12[ids[:, 12]], tbl_13[ids[:, 13]], tbl_14[ids[:, 14]], tbl_15[ids[:, 15]], tbl_16[ids[:, 16]], tbl_17[ids[:, 17]], tbl_18[ids[:, 18]], tbl_19[ids[:, 19]], tbl_20[ids[:, 20]], tbl_21[ids[:, 21]], tbl_22[ids[:, 22]], tbl_23[ids[:, 23]], tbl_24[ids[:, 24]], tbl_25[ids[:, 25]]], axis=1)
    z = _L0_rec_ref(r_dense_features, e)
    z = z.reshape(z.shape[0], -1)
    h = jnp.concatenate([z, r_dense_features], axis=1)
    h = jnp.maximum(h @ W_top1 + b_top1, 0.0)
    h = jnp.maximum(h @ W_top2 + b_top2, 0.0)
    y = h @ W_top3
    return y

_drawn_inputs = setup_inputs


def setup_inputs(seed=0):
    import zlib

    import numpy as np

    out = dict(_drawn_inputs(seed))
    spreads = {'b_top1': (0.0, 0.1), 'b_top2': (0.0, 0.1)}
    factors = {}
    for name, (base, spread) in spreads.items():
        noise = np.random.default_rng([zlib.crc32(name.encode()), seed]).standard_normal(out[name].shape)
        drawn = base * np.exp(spread * noise) if base else spread * noise
        out[name] = jnp.asarray(drawn.astype(out[name].dtype))
    for name, factor in factors.items():
        out[name] = (out[name] * factor).astype(out[name].dtype)
    return out
```

```python
import concourse.bass as bass
from concourse import mybir
from contextlib import ExitStack

N_TABLES = 26
NF = N_TABLES + 1
B, D = 512, 128
P = 128
TILES = B // P
H1, H2 = 512, 256
ROWS = [12500, 12500, 125000, 12500, 1000, 12500, 1000, 1250, 1250, 12500, 1250, 1000, 12500, 1000, 1250, 1250,
        12500, 1000, 12500, 1250, 1000, 1250, 1250, 1250, 1250, 1000]
SMALL = [4, 6, 11, 13, 17, 20, 25, 7]
GATHERED = [t for t in range(N_TABLES) if t not in SMALL]
TP_ROWS = 125
MAX_CHUNKS = max(ROWS[t] for t in SMALL) // TP_ROWS
ORDER = [0] + [t + 1 for t in GATHERED] + [t + 1 for t in SMALL]
POS_GATHERED, POS_SMALL = 1, 1 + len(GATHERED)
GROUP = 4
GROUPS = [(g, min(g + GROUP, len(GATHERED))) for g in range(0, len(GATHERED), GROUP)]

DIAGS = (NF - 1) // 2
PAIRS = DIAGS * NF
CHUNKS = 3
CHUNK = PAIRS // CHUNKS
SQ = 32
SPAN = NF + DIAGS


def pair_rows():
    rows = []
    for d in range(1, DIAGS + 1):
        for f in range(NF):
            i, j = sorted((ORDER[f], ORDER[(f + d) % NF]))
            rows.append(D + i * NF - i * (i + 1) // 2 + (j - i - 1))
    return rows


def dlrm_tower(nc, ids, ids_t, dense, tables, w_dense, w_pairs, b1, w2, b2, w3, ident_in, rownum_in, out):
    fp32, fp32r, i32, u32 = mybir.dt.float32, mybir.dt.float32r, mybir.dt.int32, mybir.dt.uint32
    ALU, ACT = mybir.AluOpType, mybir.ActivationFunctionType
    K = len(SMALL)
    NG = len(GATHERED)
    RAWS, SPLITS, HOTS = 3, 2, 6

    with ExitStack() as ctx:
        def sb(name, shape, dt=fp32):
            return ctx.enter_context(nc.sbuf_tensor(name, shape, dt))

        def ps(name, shape):
            return ctx.enter_context(nc.psum_tensor(name, shape, fp32))

        def sem(name):
            return ctx.enter_context(nc.semaphore(name))

        idx = sb("idx", [P, TILES, N_TABLES], i32)
        ident = sb("ident", [P, P])
        rownum = sb("rownum", [TP_ROWS, 2 * MAX_CHUNKS])
        ids_rep = sb("ids_rep", [TP_ROWS, K, B], i32)
        raw = sb("raw", [TP_ROWS, RAWS, MAX_CHUNKS * D])
        hi = sb("hi", [TP_ROWS, SPLITS, MAX_CHUNKS * D], fp32r)
        lo = sb("lo", [TP_ROWS, SPLITS, MAX_CHUNKS * D], fp32r)
        hot = sb("hot", [TP_ROWS, HOTS, B], fp32r)
        rows = sb("rows", [P, TILES, NG, D])
        dense_sb = sb("dense_sb", [P, TILES, D])
        dense_t = sb("dense_t", [D, B])
        feat = sb("feat", [D, B, NF])
        gram_t = sb("gram_t", [P, SPAN * SQ])
        pairs_s = sb("pairs_s", [P, 2, PAIRS])
        pairs = sb("pairs", [P, 2, CHUNKS, P])
        wd = sb("wd", [P, 2, H1])
        wds = sb("wds", [P, H1])
        wp = sb("wp", [CHUNK + 1, CHUNKS, H1])
        w2_sb = sb("w2_sb", [P, H1 // P, H2])
        b2_sb = sb("b2_sb", [P, H2 // P])
        w3_sb = sb("w3_sb", [P, H2 // P])
        h1 = sb("h1", [P, H1 // P * P])
        h2 = sb("h2", [P, H2 // P * P])
        y = sb("y", [1, B])

        turn_ps = ps("turn_ps", [P, 2, 4 * P])
        gram_a = ps("gram_a", [P, SQ * SQ])
        gram_b = ps("gram_b", [P, SQ * SQ])
        pair_ps = ps("pair_ps", [P, 4 * P])
        mlp_ps = ps("mlp_ps", [P, 4 * P])
        look_ps = gram_b[:, :].rearrange("p (k b) -> p k b", k=2)
        gram_ps = [gram_a, gram_b]

        idx_in = sem("idx_in")
        const_in = sem("const_in")
        dense_in = sem("dense_in")
        weights_in = sem("weights_in")
        rep_in = sem("rep_in")
        table_in = [sem(f"table_in{k}") for k in range(K)]
        rows_in = [[sem(f"rows_in{t}_{g}") for g in range(len(GROUPS))] for t in range(TILES)]
        hi_done = sem("hi_done")
        lo_done = sem("lo_done")
        hot_done = sem("hot_done")
        hot_used = sem("hot_used")
        look_done = sem("look_done")
        look_out = sem("look_out")
        turn_done = sem("turn_done")
        turn_out = sem("turn_out")
        dense_out = sem("dense_out")
        fill_done = sem("fill_done")
        wsum_done = sem("wsum_done")
        gram_done = sem("gram_done")
        gram_out = sem("gram_out")
        picked = sem("picked")
        pair_done = sem("pair_done")
        pair_out = sem("pair_out")
        h1_done, h1_out = sem("h1_done"), sem("h1_out")
        h2_done, h2_out = sem("h2_done"), sem("h2_out")
        y_done, y_out = sem("y_done"), sem("y_out")
        stored = sem("stored")

        def chunks(k):
            return ROWS[SMALL[k]] // TP_ROWS

        CHUNKS_BEFORE = [sum(chunks(i) for i in range(k)) for k in range(K + 1)]

        NGR = len(GROUPS)
        READY_AFTER = 2

        def groups_after_table(k):
            n = k - READY_AFTER
            return [n] if 0 <= n < NGR * TILES else []

        done_early = sum(len(groups_after_table(k)) for k in range(K))

        def groups_before_gram(t):
            return [n for n in range(NGR * t, NGR * (t + 1)) if n >= done_early]

        block = ctx.enter_context(nc.Block())

        @block.sync
        def _(sp):
            def load_table(k):
                c = chunks(k)
                sp.dma_start(raw[:, k % RAWS, 0:c * D],
                             tables[SMALL[k]].rearrange("(p c) d -> p (c d)", c=c)).then_inc(table_in[k], 16)

            sp.dma_start(idx[:], ids.rearrange("(t p) f -> p t f", p=P)).then_inc(idx_in, 16)
            load_table(0)
            sp.dma_start(rownum[:], rownum_in).then_inc(rep_in, 16)
            for k, t in enumerate(SMALL):
                sp.dma_start(ids_rep[:, k, :], ids_t[t:t + 1, :].to_broadcast([TP_ROWS, B])).then_inc(rep_in, 16)
            load_table(1)
            sp.dma_start(ident[:], ident_in).then_inc(const_in, 16)
            sp.dma_start(dense_sb[:], dense.rearrange("(t p) d -> p t d", p=P)).then_inc(dense_in, 16)
            load_table(2)
            for k in range(RAWS, K):
                sp.wait_ge(lo_done, k - RAWS + 1)
                load_table(k)
            sp.dma_start(wd[:], w_dense.rearrange("(a p) n -> p a n", p=P)).then_inc(weights_in, 16)
            sp.dma_start(wp[0:CHUNK, :, :], w_pairs.rearrange("(c p) n -> p c n", p=CHUNK)).then_inc(weights_in, 16)
            sp.dma_start(wp[CHUNK:CHUNK + 1, 0, :], b1.rearrange("(a n) -> a n", a=1)).then_inc(weights_in, 16)
            sp.dma_start(w2_sb[:], w2.rearrange("(k p) n -> p k n", p=P)).then_inc(weights_in, 16)
            sp.dma_start(b2_sb[:], b2.rearrange("(p k) -> p k", k=H2 // P)).then_inc(weights_in, 16)
            sp.dma_start(w3_sb[:], w3.rearrange("(p k) o -> p (k o)", k=H2 // P)).then_inc(weights_in, 16)
            sp.wait_ge(y_out, TILES)
            sp.dma_start(out.rearrange("b o -> o b"), y[:]).then_inc(stored, 16)
            sp.wait_ge(stored, 16)

        WEIGHT_LOADS = 6

        @block.gpsimd
        def _(pool):
            pool.wait_ge(idx_in, 16)
            for t in range(TILES):
                for g, (lo_f, hi_f) in enumerate(GROUPS):
                    for f in range(lo_f, hi_f):
                        tab = GATHERED[f]
                        nc.gpsimd.indirect_dma_start(
                            rows[:, t, f, :], None, tables[tab][:, :],
                            bass.IndirectOffsetOnAxis(ap=idx[:, t, tab:tab + 1].bitcast(u32), axis=0),
                        ).then_inc(rows_in[t][g], 16)

        @block.tensor
        def _(pe):
            def transpose_dense():
                pe.wait_ge(const_in, 16)
                pe.wait_ge(dense_in, 16)
                for t in range(TILES):
                    last = nc.tensor.transpose(turn_ps[:, 0, t * P:(t + 1) * P], dense_sb[:, t, :], ident[:])
                last.then_inc(turn_done, 1)

            def transpose_group(n):
                t, g = divmod(n, NGR)
                f0, f1 = GROUPS[g]
                pe.wait_ge(rows_in[t][g], 16 * (f1 - f0))
                if n >= 1:
                    pe.wait_ge(turn_out, n)
                for f in range(f0, f1):
                    last = nc.tensor.transpose(turn_ps[:, (n + 1) % 2, (f - f0) * P:(f - f0 + 1) * P],
                                               rows[:, t, f, :], ident[:])
                last.then_inc(turn_done, 1)

            def look_up(k):
                pe.wait_ge(hi_done, k + 1)
                pe.wait_ge(lo_done, k + 1)
                if k >= 2:
                    pe.wait_ge(look_out, k - 1)
                for c in range(chunks(k)):
                    n = CHUNKS_BEFORE[k] + c
                    pe.wait_ge(hot_done, n + 1)
                    nc.tensor.matmul(look_ps[:, k % 2, :], hi[:, k % SPLITS, c * D:(c + 1) * D],
                                     hot[:, n % HOTS, :], start=(c == 0), stop=False)
                    last = nc.tensor.matmul(look_ps[:, k % 2, :], lo[:, k % SPLITS, c * D:(c + 1) * D],
                                            hot[:, n % HOTS, :], start=False, stop=(c == chunks(k) - 1))
                    last.then_inc(hot_used, 1)

            def gram(t):
                pe.wait_ge(turn_out, 1 + NGR * (t + 1))
                pe.wait_ge(look_out, K)
                if t == 0:
                    pe.wait_ge(fill_done, 1)
                if t >= 2:
                    pe.wait_ge(gram_out, t - 1)
                for s in range(SQ):
                    for j in range(P // SQ):
                        b = t * P + j * SQ + s
                        last = nc.tensor.matmul(gram_ps[t % 2][j * SQ:j * SQ + NF, s * SQ:s * SQ + NF],
                                                feat[:, b, :], feat[:, b, :], start=True, stop=True)
                last.then_inc(gram_done, 1)

            def turn_pairs(t):
                pe.wait_ge(picked, t + 1)
                if t >= 1:
                    pe.wait_ge(pair_out, t)
                for c in range(CHUNKS):
                    last = nc.tensor.transpose(pair_ps[0:CHUNK, c * P:(c + 1) * P],
                                               pairs_s[:, t % 2, c * CHUNK:(c + 1) * CHUNK], ident[:])
                last.then_inc(pair_done, 1)

            def mlp(t):
                if t == 0:
                    pe.wait_ge(weights_in, 16 * WEIGHT_LOADS)
                    pe.wait_ge(wsum_done, 1)
                    pe.wait_ge(dense_out, 1)
                else:
                    pe.wait_ge(y_out, t)
                pe.wait_ge(pair_out, t + 1)
                for m in range(H1 // P):
                    o = mlp_ps[:, m * P:(m + 1) * P]
                    cols = slice(m * P, (m + 1) * P)
                    nc.tensor.matmul(o, wds[:, cols], dense_t[:, t * P:(t + 1) * P], start=True, stop=False)
                    for c in range(CHUNKS):
                        k = CHUNK + 1 if c == 0 else CHUNK
                        last = nc.tensor.matmul(o, wp[0:k, c, cols], pairs[0:k, t % 2, c, :],
                                                start=False, stop=(c == CHUNKS - 1))
                last.then_inc(h1_done, 1)
                pe.wait_ge(h1_out, t + 1)
                for m in range(H2 // P):
                    for k in range(H1 // P):
                        w = w2_sb[:, k, :].rearrange("p (q m) -> p m q", m=H2 // P)[:, m, :]
                        last = nc.tensor.matmul(mlp_ps[:, m * P:(m + 1) * P], w, h1[:, k * P:(k + 1) * P],
                                                start=(k == 0), stop=(k == H1 // P - 1))
                last.then_inc(h2_done, 1)
                pe.wait_ge(h2_out, t + 1)
                for k in range(H2 // P):
                    last = nc.tensor.matmul(mlp_ps[0:1, 0:P], w3_sb[:, k:k + 1], h2[:, k * P:(k + 1) * P],
                                            start=(k == 0), stop=(k == H2 // P - 1))
                last.then_inc(y_done, 1)

            transpose_dense()
            for k in range(K):
                look_up(k)
                for n in groups_after_table(k):
                    transpose_group(n)
            last_t = TILES - 1
            for t in range(TILES):
                if t == last_t:
                    for n in groups_before_gram(t)[:-1]:
                        transpose_group(n)
                    turn_pairs(t - 1)
                    mlp(t - 1)
                    transpose_group(groups_before_gram(t)[-1])
                    gram(t)
                else:
                    for n in groups_before_gram(t):
                        transpose_group(n)
                    gram(t)
                    if t >= 1:
                        turn_pairs(t - 1)
                        mlp(t - 1)
            turn_pairs(last_t)
            mlp(last_t)

        @block.scalar
        def _(act):
            def copy_dense():
                act.wait_ge(turn_done, 1)
                nc.scalar.copy(dense_t[:], turn_ps[:, 0, :]).then_inc(dense_out, 1)
                nc.scalar.copy(feat[:, :, 0], turn_ps[:, 0, :]).then_inc(turn_out, 1)

            def copy_group(n):
                t, g = divmod(n, NGR)
                f0, f1 = GROUPS[g]
                act.wait_ge(turn_done, n + 2)
                nc.scalar.copy(feat[:, t * P:(t + 1) * P, POS_GATHERED + f0:POS_GATHERED + f1],
                               turn_ps[:, (n + 1) % 2, 0:(f1 - f0) * P].rearrange("p (f b) -> p b f", f=f1 - f0),
                               ).then_inc(turn_out, 1)

            def split_high(k):
                act.wait_ge(table_in[k], 16)
                if k >= SPLITS:
                    act.wait_ge(hot_used, CHUNKS_BEFORE[k - SPLITS + 1])
                w = chunks(k) * D
                nc.scalar.copy(hi[:, k % SPLITS, 0:w], raw[:, k % RAWS, 0:w]).then_inc(hi_done, 1)

            def copy_lookups(k):
                act.wait_ge(hot_used, CHUNKS_BEFORE[k + 1])
                nc.scalar.copy(feat[:, :, POS_SMALL + k], look_ps[:, k % 2, :]).then_inc(look_out, 1)

            def mlp(t):
                act.wait_ge(h1_done, t + 1)
                nc.scalar.activation(h1[:], mlp_ps[:], ACT.Relu).then_inc(h1_out, 1)
                act.wait_ge(h2_done, t + 1)
                for m in range(H2 // P):
                    last = nc.scalar.activation(h2[:, m * P:(m + 1) * P], mlp_ps[:, m * P:(m + 1) * P], ACT.Relu,
                                                bias=b2_sb[:, m:m + 1])
                last.then_inc(h2_out, 1)
                act.wait_ge(y_done, t + 1)
                nc.scalar.copy(y[0:1, t * P:(t + 1) * P], mlp_ps[0:1, 0:P]).then_inc(y_out, 1)

            split_high(0)
            copy_dense()
            split_high(1)
            for k in range(K):
                copy_lookups(k)
                if k + SPLITS < K:
                    split_high(k + SPLITS)
                for n in groups_after_table(k):
                    copy_group(n)
            act.wait_ge(weights_in, 16 * WEIGHT_LOADS)
            last_t = TILES - 1
            for t in range(TILES):
                if t == last_t:
                    for n in groups_before_gram(t)[:-1]:
                        copy_group(n)
                    mlp(t - 1)
                    copy_group(groups_before_gram(t)[-1])
                else:
                    for n in groups_before_gram(t):
                        copy_group(n)
                    if t >= 1:
                        mlp(t - 1)
            mlp(last_t)

        @block.vector
        def _(dve):
            def split_low(k):
                dve.wait_ge(hi_done, k + 1)
                w = chunks(k) * D
                nc.vector.tensor_tensor(lo[:, k % SPLITS, 0:w], raw[:, k % RAWS, 0:w],
                                        hi[:, k % SPLITS, 0:w].bitcast(fp32), ALU.subtract).then_inc(lo_done, 1)

            def one_hots(k):
                if k == 0:
                    dve.wait_ge(rep_in, 16 * (K + 1))
                for c in range(chunks(k)):
                    n = CHUNKS_BEFORE[k] + c
                    if n >= HOTS:
                        dve.wait_ge(hot_used, n - HOTS + 1)
                    col = c if chunks(k) == 8 else MAX_CHUNKS + c
                    nc.vector.tensor_scalar(hot[:, n % HOTS, :], ids_rep[:, k, :], rownum[:, col:col + 1], None,
                                            ALU.is_equal).then_inc(hot_done, 1)

            def turn_gram(t):
                dve.wait_ge(gram_done, t + 1)
                if t >= 1:
                    dve.wait_ge(picked, t)
                src = gram_ps[t % 2][:, :].rearrange("p (s g) -> p g s", g=SQ)
                dst = gram_t[:, :].rearrange("p (g f) -> p g f", f=SQ)
                nc.vector.transpose(dst[:, 0:NF, :], src[:, 0:NF, :])
                nc.vector.transpose(dst[:, NF:SPAN, :], src[:, 0:DIAGS, :]).then_inc(gram_out, 1)
                dve.wait_ge(gram_out, t + 1)
                if t >= 2:
                    dve.wait_ge(pair_done, t - 1)
                whole = gram_t[:, :]
                skewed = bass.AP(whole.tensor, whole.offset + SQ, [whole.ap[0], [SQ, DIAGS], [SQ + 1, NF]])
                nc.vector.tensor_copy(pairs_s[:, t % 2, :].rearrange("p (d f) -> p d f", f=NF),
                                      skewed).then_inc(picked, 1)

            def copy_pairs(t):
                dve.wait_ge(pair_done, t + 1)
                if t >= 2:
                    dve.wait_ge(h1_done, t - 1)
                nc.vector.tensor_copy(pairs[0:CHUNK, t % 2, :, :],
                                      pair_ps[0:CHUNK, 0:CHUNKS * P].rearrange("p (c b) -> p c b", c=CHUNKS),
                                      ).then_inc(pair_out, 1)

            nc.vector.memset(gram_a[:], 0.0).then_inc(fill_done, 1)
            nc.vector.memset(pairs[:], 1.0).then_inc(fill_done, 1)
            for k in range(K):
                split_low(k)
                one_hots(k)
            dve.wait_ge(fill_done, 2)
            dve.wait_ge(weights_in, 16 * WEIGHT_LOADS)
            nc.vector.tensor_tensor(wds[:], wd[:, 0, :], wd[:, 1, :], ALU.add).then_inc(wsum_done, 1)
            turn_gram(0)
            for t in range(1, TILES):
                if t == TILES - 1:
                    copy_pairs(t - 1)
                    turn_gram(t)
                else:
                    turn_gram(t)
                    copy_pairs(t - 1)
            copy_pairs(TILES - 1)


def kernel(**inputs):
    import numpy as np
    import concourse.bacc as bacc
    from concourse.bass_utils import run_bass_kernel_spmd

    nc = bacc.Bacc("TRN2", target_bir_lowering=False, num_devices=1)
    arrays = {}

    def give(name, a):
        name = "in_" + name
        a = np.ascontiguousarray(a)
        arrays[name] = a
        return nc.dram_tensor(name, a.shape, mybir.dt.from_np(a.dtype), kind="ExternalInput").ap()

    w1 = np.asarray(inputs["W_top1"])
    ids = np.asarray(inputs["ids"])
    n_pairs = CHUNKS * CHUNK
    rownum = np.concatenate([np.arange(TP_ROWS)[:, None] * c + np.arange(MAX_CHUNKS)[None, :] for c in (8, 10)], 1)
    args = [
        give("ids", ids),
        give("ids_t", ids.T),
        give("dense", inputs["r_dense_features"]),
        [give(f"tbl_{t}", inputs[f"tbl_{t}"]) for t in range(N_TABLES)],
        give("w_dense", np.concatenate([w1[0:D], w1[D + n_pairs:]], 0)),
        give("w_pairs", w1[pair_rows()]),
        give("b1", inputs["b_top1"]),
        give("w2", inputs["W_top2"]),
        give("b2", inputs["b_top2"]),
        give("w3", inputs["W_top3"]),
        give("ident", np.eye(P, dtype=np.float32)),
        give("rownum", rownum.astype(np.float32)),
    ]
    out = nc.dram_tensor("out_0", (B, 1), mybir.dt.float32, kind="ExternalOutput").ap()
    dlrm_tower(nc, *args, out)
    return run_bass_kernel_spmd(nc, [arrays], core_ids=[0]).results[0]["out_0"]
```

```python
import concourse.bass as bass
from concourse import mybir
from contextlib import ExitStack

N_TABLES = 26
NF = N_TABLES + 1
B, D = 512, 128
P = 128
TILES = B // P
H1, H2 = 512, 256
ROWS = [12500, 12500, 125000, 12500, 1000, 12500, 1000, 1250, 1250, 12500, 1250, 1000, 12500, 1000, 1250, 1250,
        12500, 1000, 12500, 1250, 1000, 1250, 1250, 1250, 1250, 1000]
SMALL = [4, 6, 11, 13, 17, 20, 25, 7, 8]
GATHERED = [t for t in range(N_TABLES) if t not in SMALL]
TP_ROWS = 125
MAX_CHUNKS = max(ROWS[t] for t in SMALL) // TP_ROWS
ORDER = [0] + [t + 1 for t in GATHERED] + [t + 1 for t in SMALL]
POS_GATHERED, POS_SMALL = 1, 1 + len(GATHERED)
NGR = -(-len(GATHERED) // 4)
GROUPS = [(4 * g, min(4 * (g + 1), len(GATHERED))) for g in range(NGR)]

DIAGS = (NF - 1) // 2
PAIRS = DIAGS * NF
CHUNKS = 3
CHUNK = PAIRS // CHUNKS
SQ = 32
SPAN = NF + DIAGS


def pair_rows():
    rows = []
    for d in range(1, DIAGS + 1):
        for f in range(NF):
            i, j = sorted((ORDER[f], ORDER[(f + d) % NF]))
            rows.append(D + i * NF - i * (i + 1) // 2 + (j - i - 1))
    return rows


def dlrm_tower(nc, ids, ids_small, dense, tables, w_dense, w_pairs, b1, w2, b2, w3, ident_src, rownum_src, out):
    fp32, fp32r, i32, u32 = mybir.dt.float32, mybir.dt.float32r, mybir.dt.int32, mybir.dt.uint32
    ALU, ACT = mybir.AluOpType, mybir.ActivationFunctionType
    K = len(SMALL)
    NG = len(GATHERED)
    RAWS, SPLITS, HOTS, ACT_HOTS = 3, 2, 6, 3

    WARM_UPS = 20

    with ExitStack() as ctx:
        def sb(name, shape, dt=fp32):
            return ctx.enter_context(nc.sbuf_tensor(name, shape, dt))

        def ps(name, shape):
            return ctx.enter_context(nc.psum_tensor(name, shape, fp32))

        def sem(name):
            return ctx.enter_context(nc.semaphore(name))

        idx = sb("idx", [P, TILES, N_TABLES], i32)
        ident = sb("ident", [P, P])
        rownum = sb("rownum", [TP_ROWS, 2 * MAX_CHUNKS])
        ids_rep = sb("ids_rep", [TP_ROWS, RAWS, B], i32)
        raw = sb("raw", [TP_ROWS, RAWS, MAX_CHUNKS * D])
        hi = sb("hi", [TP_ROWS, SPLITS, MAX_CHUNKS * D], fp32r)
        lo = sb("lo", [TP_ROWS, SPLITS, MAX_CHUNKS * D], fp32r)
        hot = sb("hot", [TP_ROWS, HOTS, B], fp32r)
        act_hot = sb("act_hot", [TP_ROWS, ACT_HOTS, B], fp32r)
        distance = sb("distance", [TP_ROWS, B])
        rows = sb("rows", [P, TILES, NG, D])
        dense_sb = sb("dense_sb", [P, TILES, D])
        dense_t = sb("dense_t", [D, B])
        feat = sb("feat", [D, B, NF])
        gram_t = sb("gram_t", [P, SPAN * SQ])
        pairs_s = sb("pairs_s", [P, 2, PAIRS])
        pairs = sb("pairs", [P, 2, CHUNKS, P])
        wd = sb("wd", [P, 2, H1])
        wds = sb("wds", [P, H1])
        wp = sb("wp", [CHUNK + 1, CHUNKS, H1])
        w2_sb = sb("w2_sb", [P, H1 // P, H2])
        b2_sb = sb("b2_sb", [P, H2 // P])
        w3_sb = sb("w3_sb", [P, H2 // P])
        h1 = sb("h1", [P, H1 // P * P])
        h2 = sb("h2", [P, H2 // P * P])
        y = sb("y", [1, B])

        warm = sb("warm", [P, 4 * P], mybir.dt.bfloat16)
        turn_ps = ps("turn_ps", [P, 2, 4 * P])
        gram_a = ps("gram_a", [P, SQ * SQ])
        gram_b = ps("gram_b", [P, SQ * SQ])
        mlp_ps = ps("mlp_ps", [P, 2, 4 * P])
        look_ps = gram_b[:, :].rearrange("p (k b) -> p k b", k=2)
        gram_ps = [gram_a, gram_b]

        idx_in = sem("idx_in")
        const_in = sem("const_in")
        dense_in = sem("dense_in")
        weights_in = sem("weights_in")
        rownum_in = sem("rownum_in")
        ids_in = [sem(f"ids_in{k}") for k in range(RAWS)]
        table_in = [sem(f"table_in{k}") for k in range(RAWS)]
        rows_in = [[sem(f"rows_in{t}_{g}") for g in range(NGR)] for t in range(TILES)]
        hi_done = sem("hi_done")
        lo_done = sem("lo_done")
        hot_done = sem("hot_done")
        hot_used = sem("hot_used")
        distance_done = sem("distance_done")
        act_hot_done = sem("act_hot_done")
        act_hot_used = sem("act_hot_used")
        look_out = sem("look_out")
        turn_done = sem("turn_done")
        turn_out = sem("turn_out")
        dense_out = sem("dense_out")
        warm_cleared = sem("warm_cleared")
        gram_cleared = sem("gram_cleared")
        ones_done = sem("ones_done")
        wsum_done = sem("wsum_done")
        gram_done = sem("gram_done")
        gram_out = sem("gram_out")
        picked = sem("picked")
        picked_act = sem("picked_act")
        gram_half = sem("gram_half")
        chunk_out = sem("chunk_out")
        h1_act, h1_dve = sem("h1_act"), sem("h1_dve")
        h2_act, h2_dve = sem("h2_act"), sem("h2_dve")
        h1_done, h1_out = sem("h1_done"), sem("h1_out")
        h2_done, h2_out = sem("h2_done"), sem("h2_out")
        y_done, y_out = sem("y_done"), sem("y_out")
        stored = sem("stored")

        def chunks(k):
            return ROWS[SMALL[k]] // TP_ROWS

        def row_column(k, c):
            return c if chunks(k) == ROWS[4] // TP_ROWS else MAX_CHUNKS + c

        def skewed_gram(first, end):
            whole = gram_t[:, :]
            return bass.AP(whole.tensor, whole.offset + SQ + (SQ + 1) * first,
                           [whole.ap[0], [SQ, DIAGS], [SQ + 1, end - first]])

        def picked_pairs(t, first, end):
            return pairs_s[:, t % 2, :].rearrange("p (d f) -> p d f", f=NF)[:, :, first:end]

        ACT_CHUNKS = [2 if k % 2 or chunks(k) == MAX_CHUNKS else 1 for k in range(K)]
        HOTS_BEFORE = [sum(chunks(i) - ACT_CHUNKS[i] for i in range(k)) for k in range(K + 1)]
        ACT_HOTS_BEFORE = [sum(ACT_CHUNKS[:k]) for k in range(K + 1)]

        EARLY = [[], [0], [1], [2], [3, 4], [5], [6], [7], [8, 9]]
        GRAM_PIECES = 8
        H1_PIECES = H1 // P
        last_t = TILES - 1

        def rows_of(first, end):
            return [("rows", n) for n in range(first, end)]

        def gram_pieces(t, first, end):
            return [("gram", (t, i)) for i in range(first, end)]

        STEPS = gram_pieces(0, 0, GRAM_PIECES) + gram_pieces(1, 0, 4) + [("pairs", 0)] + gram_pieces(1, 4, 5)
        for m in range(H1_PIECES):
            STEPS += [("hidden1", (0, m))] + (gram_pieces(1, 5 + m, 6 + m) if m < 2 else [])
        STEPS += gram_pieces(1, 7, 8) + rows_of(2 * NGR, 2 * NGR + 2) + [("hidden2", 0), ("pairs", 1)]
        STEPS += rows_of(2 * NGR + 2, 2 * NGR + 3) + [("output", 0)] + rows_of(2 * NGR + 3, 3 * NGR)
        for m in range(H1_PIECES):
            STEPS += [("hidden1", (1, m))] + gram_pieces(2, 2 * m, 2 * m + 2)
        STEPS += rows_of(3 * NGR, 3 * NGR + 1) + [("hidden2", 1), ("pairs", 2), ("output", 1)]
        STEPS += rows_of(3 * NGR + 1, 4 * NGR)
        for m in range(H1_PIECES):
            STEPS += [("hidden1", (2, m))] + gram_pieces(3, 2 * m, 2 * m + 2)
        STEPS += [("pick", 3), ("hidden2", 2), ("pairs", 3), ("output", 2), ("finish", 3)]

        JOBS = [("dense", 0)] + [("rows", n) for e in EARLY for n in e]
        JOBS += [step for step in STEPS if step[0] in ("rows", "pairs")]
        JOB = {job: i for i, job in enumerate(JOBS)}
        wide_ps = [mlp_ps[:, 1, 0:P], gram_a[:, 0:P], gram_a[:, 4 * P:5 * P],
                   turn_ps[:, (JOB["pairs", last_t] + 1) % 2, 0:P]]

        block = ctx.enter_context(nc.Block())

        @block.sync
        def _(sp):
            def load_table(k):
                c = chunks(k)
                if k >= RAWS:
                    sp.wait_ge(lo_done, k - RAWS + 1)
                    sp.wait_ge(hot_done, HOTS_BEFORE[k - RAWS + 1])
                    sp.wait_ge(distance_done, ACT_HOTS_BEFORE[k - RAWS + 1])
                sp.dma_start(ids_rep[:, k % RAWS, :], ids_small[k:k + 1, :].to_broadcast([TP_ROWS, B])
                             ).then_inc(ids_in[k % RAWS], 16)
                sp.dma_start(raw[:, k % RAWS, 0:c * D],
                             tables[SMALL[k]].rearrange("(p c) d -> p (c d)", c=c)).then_inc(table_in[k % RAWS], 16)

            sp.dma_start(idx[:], ids.rearrange("(t p) f -> p t f", p=P)).then_inc(idx_in, 16)
            sp.dma_start(rownum[:], rownum_src).then_inc(rownum_in, 16)
            load_table(0)
            load_table(1)
            sp.dma_start(ident[:], ident_src).then_inc(const_in, 16)
            sp.dma_start(dense_sb[:], dense.rearrange("(t p) d -> p t d", p=P)).then_inc(dense_in, 16)
            for k in range(2, K):
                load_table(k)
            sp.dma_start(wd[:], w_dense.rearrange("(a p) n -> p a n", p=P)).then_inc(weights_in, 16)
            sp.dma_start(wp[0:CHUNK, :, :], w_pairs.rearrange("(c p) n -> p c n", p=CHUNK)).then_inc(weights_in, 16)
            sp.dma_start(wp[CHUNK:CHUNK + 1, 0, :], b1.rearrange("(a n) -> a n", a=1)).then_inc(weights_in, 16)
            sp.dma_start(w2_sb[:], w2.rearrange("(k p) n -> p k n", p=P)).then_inc(weights_in, 16)
            sp.dma_start(b2_sb[:], b2.rearrange("(p k) -> p k", k=H2 // P)).then_inc(weights_in, 16)
            sp.dma_start(w3_sb[:], w3.rearrange("(p k) o -> p (k o)", k=H2 // P)).then_inc(weights_in, 16)
            sp.wait_ge(y_out, TILES)
            sp.dma_start(out.rearrange("b o -> o b"), y[:]).then_inc(stored, 16)
            sp.wait_ge(stored, 16)

        WEIGHT_LOADS = 6

        @block.gpsimd
        def _(pool):
            nc.gpsimd.memset(pairs[:], 1.0).then_inc(ones_done, 1)
            pool.wait_ge(idx_in, 16)
            for t in range(TILES):
                for g, (lo_f, hi_f) in enumerate(GROUPS):
                    for f in range(lo_f, hi_f):
                        tab = GATHERED[f]
                        nc.gpsimd.indirect_dma_start(
                            rows[:, t, f, :], None, tables[tab][:, :],
                            bass.IndirectOffsetOnAxis(ap=idx[:, t, tab:tab + 1].bitcast(u32), axis=0),
                        ).then_inc(rows_in[t][g], 16)

        @block.tensor
        def _(pe):
            def transpose_dense():
                pe.wait_ge(const_in, 16)
                pe.wait_ge(dense_in, 16)
                for t in range(TILES):
                    last = nc.tensor.transpose(turn_ps[:, 0, t * P:(t + 1) * P], dense_sb[:, t, :], ident[:])
                last.then_inc(turn_done, 1)

            def transpose_group(n):
                job = JOB["rows", n]
                t, g = divmod(n, NGR)
                f0, f1 = GROUPS[g]
                pe.wait_ge(rows_in[t][g], 16 * (f1 - f0))
                if job >= 2:
                    pe.wait_ge(turn_out, job - 1)
                for f in range(f0, f1):
                    last = nc.tensor.transpose(turn_ps[:, job % 2, (f - f0) * P:(f - f0 + 1) * P],
                                               rows[:, t, f, :], ident[:])
                last.then_inc(turn_done, 1)

            def look_up(k):
                pe.wait_ge(lo_done, k + 1)
                if k >= 2:
                    pe.wait_ge(look_out, k - 1)
                for c in range(chunks(k)):
                    if c < chunks(k) - ACT_CHUNKS[k]:
                        n = HOTS_BEFORE[k] + c
                        pe.wait_ge(hot_done, n + 1)
                        one_hot, used = hot[:, n % HOTS, :], hot_used
                    else:
                        n = ACT_HOTS_BEFORE[k] + c - (chunks(k) - ACT_CHUNKS[k])
                        pe.wait_ge(act_hot_done, n + 1)
                        one_hot, used = act_hot[:, n % ACT_HOTS, :], act_hot_used
                    nc.tensor.matmul(look_ps[:, k % 2, :], hi[:, k % SPLITS, c * D:(c + 1) * D],
                                     one_hot, start=(c == 0), stop=False)
                    nc.tensor.matmul(look_ps[:, k % 2, :], lo[:, k % SPLITS, c * D:(c + 1) * D],
                                     one_hot, start=False, stop=(c == chunks(k) - 1)).then_inc(used, 1)

            def gram(t, piece):
                if piece == 0:
                    pe.wait_ge(turn_out, JOB["rows", NGR * (t + 1) - 1] + 1)
                    pe.wait_ge(look_out, K)
                    if t == 0:
                        pe.wait_ge(gram_cleared, 1)
                    if t >= 2:
                        pe.wait_ge(gram_out, t - 1)
                for s in range(piece * SQ // GRAM_PIECES, (piece + 1) * SQ // GRAM_PIECES):
                    for j in range(P // SQ):
                        b = t * P + j * SQ + s
                        last = nc.tensor.matmul(gram_ps[t % 2][j * SQ:j * SQ + NF, s * SQ:s * SQ + NF],
                                                feat[:, b, :], feat[:, b, :], start=True, stop=True)
                if piece == GRAM_PIECES - 1:
                    last.then_inc(gram_done, 1)

            def turn_pairs(t):
                job = JOB["pairs", t]
                pe.wait_ge(picked, t + 1)
                if t == last_t:
                    pe.wait_ge(picked_act, 1)
                pe.wait_ge(turn_out, job - 1)
                for c in range(CHUNKS):
                    last = nc.tensor.transpose(turn_ps[0:CHUNK, job % 2, c * P:(c + 1) * P],
                                               pairs_s[:, t % 2, c * CHUNK:(c + 1) * CHUNK], ident[:])
                last.then_inc(turn_done, 1)

            def hidden1(t, m):
                if m == 0:
                    if t == 0:
                        pe.wait_ge(weights_in, 16 * WEIGHT_LOADS)
                        pe.wait_ge(wsum_done, 1)
                        pe.wait_ge(dense_out, 1)
                    if t >= 2:
                        pe.wait_ge(y_out, t - 1)
                    pe.wait_ge(turn_out, JOB["pairs", t] + 1)
                o = mlp_ps[:, t % 2, m * P:(m + 1) * P]
                cols = slice(m * P, (m + 1) * P)
                nc.tensor.matmul(o, wds[:, cols], dense_t[:, t * P:(t + 1) * P], start=True, stop=False)
                for c in range(CHUNKS):
                    k = CHUNK + 1 if c == 0 else CHUNK
                    last = nc.tensor.matmul(o, wp[0:k, c, cols], pairs[0:k, t % 2, c, :],
                                            start=False, stop=(c == CHUNKS - 1))
                if m == H1_PIECES - 1:
                    last.then_inc(h1_done, 1)

            def hidden2(t):
                pe.wait_ge(h1_out, t + 1)
                for m in range(H2 // P):
                    for k in range(H1 // P):
                        w = w2_sb[:, k, :].rearrange("p (q m) -> p m q", m=H2 // P)[:, m, :]
                        last = nc.tensor.matmul(mlp_ps[:, t % 2, m * P:(m + 1) * P], w, h1[:, k * P:(k + 1) * P],
                                                start=(k == 0), stop=(k == H1 // P - 1))
                last.then_inc(h2_done, 1)

            def finish(t):
                for c in range(CHUNKS):
                    pe.wait_ge(chunk_out, c + 1)
                    for m in range(H1_PIECES):
                        k = CHUNK + 1 if c == 0 else CHUNK
                        last = nc.tensor.matmul(wide_ps[m], wp[0:k, c, m * P:(m + 1) * P], pairs[0:k, t % 2, c, :],
                                                start=False, stop=(c == CHUNKS - 1))
                        if c == CHUNKS - 1:
                            last.then_inc(h1_done, 1)
                for k in range(H1_PIECES):
                    if k % 2 == 0:
                        pe.wait_ge(h1_dve, k // 2 + 1)
                    else:
                        pe.wait_ge(h1_act, k // 2 + 1)
                    for m in range(H2 // P):
                        w = w2_sb[:, k, :].rearrange("p (q m) -> p m q", m=H2 // P)[:, m, :]
                        last = nc.tensor.matmul(gram_b[:, m * 4 * P:m * 4 * P + P], w, h1[:, k * P:(k + 1) * P],
                                                start=(k == 0), stop=(k == H1_PIECES - 1))
                        if k == H1_PIECES - 1:
                            last.then_inc(h2_done, 1)
                pe.wait_ge(y_out, t)
                for k in range(H2 // P):
                    if k == 0:
                        pe.wait_ge(h2_act, 1)
                    else:
                        pe.wait_ge(h2_dve, 1)
                    last = nc.tensor.matmul(mlp_ps[0:1, 0, 0:P], w3_sb[:, k:k + 1], h2[:, k * P:(k + 1) * P],
                                            start=(k == 0), stop=(k == H2 // P - 1))
                last.then_inc(y_done, 1)

            def finish_dense(t):
                pe.wait_ge(y_out, t - 1)
                pe.wait_ge(gram_out, t)
                pe.wait_ge(turn_out, JOB["pairs", t])
                for m in range(H1_PIECES):
                    nc.tensor.matmul(wide_ps[m], wds[:, m * P:(m + 1) * P], dense_t[:, t * P:(t + 1) * P],
                                     start=True, stop=False)

            def output(t):
                pe.wait_ge(h2_out, t + 1)
                for k in range(H2 // P):
                    last = nc.tensor.matmul(mlp_ps[0:1, t % 2, 0:P], w3_sb[:, k:k + 1], h2[:, k * P:(k + 1) * P],
                                            start=(k == 0), stop=(k == H2 // P - 1))
                last.then_inc(y_done, 1)

            pe.wait_ge(warm_cleared, 1)
            for i in range(WARM_UPS):
                nc.tensor.matmul(turn_ps[:, 0, :], warm[:, 0:P], warm[:], start=True, stop=True)
            for k in range(K):
                look_up(k)
                if k == 0:
                    transpose_dense()
                for n in EARLY[k]:
                    transpose_group(n)
            for step, n in STEPS:
                if step == "rows":
                    transpose_group(n)
                elif step == "gram":
                    gram(*n)
                elif step == "hidden1":
                    hidden1(*n)
                elif step == "pairs":
                    if n == last_t:
                        finish_dense(n)
                    turn_pairs(n)
                elif step == "hidden2":
                    hidden2(n)
                elif step == "output":
                    output(n)
                elif step == "finish":
                    finish(n)

        @block.scalar
        def _(act):
            def copy_dense():
                act.wait_ge(turn_done, 1)
                nc.scalar.copy(dense_t[:], turn_ps[:, 0, :]).then_inc(dense_out, 1)
                nc.scalar.copy(feat[:, :, 0], turn_ps[:, 0, :]).then_inc(turn_out, 1)

            def copy_group(n):
                job = JOB["rows", n]
                t, g = divmod(n, NGR)
                f0, f1 = GROUPS[g]
                act.wait_ge(turn_done, job + 1)
                nc.scalar.copy(feat[:, t * P:(t + 1) * P, POS_GATHERED + f0:POS_GATHERED + f1],
                               turn_ps[:, job % 2, 0:(f1 - f0) * P].rearrange("p (f b) -> p b f", f=f1 - f0),
                               ).then_inc(turn_out, 1)

            def split_high(k):
                act.wait_ge(table_in[k % RAWS], 16 * (k // RAWS + 1))
                if k >= SPLITS:
                    act.wait_ge(act_hot_used, ACT_HOTS_BEFORE[k - SPLITS + 1])
                w = chunks(k) * D
                nc.scalar.copy(hi[:, k % SPLITS, 0:w], raw[:, k % RAWS, 0:w]).then_inc(hi_done, 1)

            def act_one_hots(k):
                if k == 0:
                    act.wait_ge(rownum_in, 16)
                act.wait_ge(ids_in[k % RAWS], 16 * (k // RAWS + 1))
                for i in range(ACT_CHUNKS[k]):
                    n = ACT_HOTS_BEFORE[k] + i
                    col = row_column(k, chunks(k) - ACT_CHUNKS[k] + i)
                    if n >= 1:
                        act.wait_ge(act_hot_done, n)
                    nc.scalar.activation(distance[:], ids_rep[:, k % RAWS, :], ACT.Abs, scale=-1.0,
                                         bias=rownum[:, col:col + 1]).then_inc(distance_done, 1)
                    act.wait_ge(distance_done, n + 1)
                    if n >= ACT_HOTS:
                        act.wait_ge(act_hot_used, n - ACT_HOTS + 1)
                    nc.scalar.activation(act_hot[:, n % ACT_HOTS, :], distance[:], ACT.Relu, scale=-1.0,
                                         bias=1.0).then_inc(act_hot_done, 1)

            def copy_lookups(k):
                act.wait_ge(act_hot_used, ACT_HOTS_BEFORE[k + 1])
                nc.scalar.copy(feat[:, :, POS_SMALL + k], look_ps[:, k % 2, :]).then_inc(look_out, 1)

            def copy_pairs(t):
                job = JOB["pairs", t]
                act.wait_ge(turn_done, job + 1)
                if t == 0:
                    act.wait_ge(ones_done, 1)
                if t >= 2:
                    act.wait_ge(h1_done, t - 1)
                if t == last_t:
                    for c in range(CHUNKS):
                        nc.scalar.copy(pairs[0:CHUNK, t % 2, c, :],
                                       turn_ps[0:CHUNK, job % 2, c * P:(c + 1) * P]).then_inc(chunk_out, 1)
                    return
                nc.scalar.copy(pairs[0:CHUNK, t % 2, :, :],
                               turn_ps[0:CHUNK, job % 2, 0:CHUNKS * P].rearrange("p (c b) -> p c b", c=CHUNKS),
                               ).then_inc(turn_out, 1)

            def relu2(t):
                act.wait_ge(h2_done, t + 1)
                if t >= 1:
                    act.wait_ge(y_done, t)
                for m in range(H2 // P):
                    last = nc.scalar.activation(h2[:, m * P:(m + 1) * P], mlp_ps[:, t % 2, m * P:(m + 1) * P],
                                                ACT.Relu, bias=b2_sb[:, m:m + 1])
                last.then_inc(h2_out, 1)

            def pick_first(t):
                act.wait_ge(gram_half, t + 1)
                act.wait_ge(turn_done, JOB["pairs", t - 2] + 1)
                nc.scalar.copy(picked_pairs(t, 0, NF - DIAGS), skewed_gram(0, NF - DIAGS)).then_inc(picked_act, 1)

            def finish(t):
                act.wait_ge(h2_done, t)
                for m in (1, 3):
                    act.wait_ge(h1_done, t + m + 1)
                    nc.scalar.activation(h1[:, m * P:(m + 1) * P], wide_ps[m], ACT.Relu).then_inc(h1_act, 1)
                act.wait_ge(y_done, t)
                act.wait_ge(h2_done, t + 1)
                nc.scalar.activation(h2[:, 0:P], gram_b[:, 0:P], ACT.Relu, bias=b2_sb[:, 0:1]).then_inc(h2_act, 1)
                act.wait_ge(y_done, t + 1)
                nc.scalar.copy(y[0:1, t * P:(t + 1) * P], mlp_ps[0:1, 0, 0:P]).then_inc(y_out, 1)

            def copy_output(t):
                act.wait_ge(y_done, t + 1)
                nc.scalar.copy(y[0:1, t * P:(t + 1) * P], mlp_ps[0:1, t % 2, 0:P]).then_inc(y_out, 1)

            split_high(0)
            act_one_hots(0)
            for k in range(K):
                if k + 1 < K:
                    split_high(k + 1)
                    act_one_hots(k + 1)
                copy_lookups(k)
                if k == 0:
                    copy_dense()
                for n in EARLY[k]:
                    copy_group(n)
            act.wait_ge(weights_in, 16 * WEIGHT_LOADS)
            for step, n in STEPS:
                if step == "rows":
                    copy_group(n)
                elif step == "pick":
                    pick_first(n)
                elif step == "pairs":
                    copy_pairs(n)
                elif step == "hidden2":
                    relu2(n)
                elif step == "output":
                    copy_output(n)
                elif step == "finish":
                    finish(n)

        @block.vector
        def _(dve):
            def split_low(k):
                dve.wait_ge(hi_done, k + 1)
                w = chunks(k) * D
                nc.vector.tensor_tensor(lo[:, k % SPLITS, 0:w], raw[:, k % RAWS, 0:w],
                                        hi[:, k % SPLITS, 0:w].bitcast(fp32), ALU.subtract).then_inc(lo_done, 1)

            def one_hots(k, c0, c1):
                if k == 0:
                    dve.wait_ge(rownum_in, 16)
                dve.wait_ge(ids_in[k % RAWS], 16 * (k // RAWS + 1))
                for c in range(c0, c1):
                    n = HOTS_BEFORE[k] + c
                    if n >= HOTS:
                        dve.wait_ge(hot_used, n - HOTS + 1)
                    col = row_column(k, c)
                    nc.vector.tensor_scalar(hot[:, n % HOTS, :], ids_rep[:, k % RAWS, :], rownum[:, col:col + 1],
                                            None, ALU.is_equal).then_inc(hot_done, 1)

            def turn_gram(t):
                dve.wait_ge(gram_done, t + 1)
                if t >= 1:
                    dve.wait_ge(picked, t)
                src = gram_ps[t % 2][:, :].rearrange("p (s g) -> p g s", g=SQ)
                dst = gram_t[:, :].rearrange("p (g f) -> p g f", f=SQ)
                nc.vector.transpose(dst[:, 0:NF, :], src[:, 0:NF, :]).then_inc(gram_half, 1)
                nc.vector.transpose(dst[:, NF:SPAN, :], src[:, 0:DIAGS, :]).then_inc(gram_out, 1)
                dve.wait_ge(gram_out, t + 1)
                if t >= 2:
                    dve.wait_ge(turn_done, JOB["pairs", t - 2] + 1)
                first = NF - DIAGS if t == last_t else 0
                nc.vector.tensor_copy(picked_pairs(t, first, NF), skewed_gram(first, NF)).then_inc(picked, 1)

            def relu1(t):
                dve.wait_ge(h1_done, t + 1)
                if t >= 1:
                    dve.wait_ge(h2_done, t)
                nc.vector.tensor_scalar(h1[:], mlp_ps[:, t % 2, :], 0.0, None, ALU.max).then_inc(h1_out, 1)

            def finish(t):
                dve.wait_ge(h2_done, t)
                for m in (0, 2):
                    dve.wait_ge(h1_done, t + m + 1)
                    nc.vector.tensor_scalar(h1[:, m * P:(m + 1) * P], wide_ps[m], 0.0, None,
                                            ALU.max).then_inc(h1_dve, 1)
                dve.wait_ge(y_done, t)
                dve.wait_ge(h2_done, t + 2)
                nc.vector.tensor_scalar(h2[:, P:2 * P], gram_b[:, 4 * P:5 * P], b2_sb[:, 1:2], 0.0,
                                        ALU.add, ALU.max).then_inc(h2_dve, 1)

            nc.vector.memset(warm[:].bitcast(u32), 0).then_inc(warm_cleared, 1)
            nc.vector.memset(gram_a[:], 0.0).then_inc(gram_cleared, 1)
            one_hots(0, 0, HOTS - 1)
            split_low(0)
            one_hots(0, HOTS - 1, chunks(0) - ACT_CHUNKS[0])
            for k in range(1, K):
                split_low(k)
                one_hots(k, 0, chunks(k) - ACT_CHUNKS[k])
            dve.wait_ge(weights_in, 16 * WEIGHT_LOADS)
            nc.vector.tensor_tensor(wds[:], wd[:, 0, :], wd[:, 1, :], ALU.add).then_inc(wsum_done, 1)
            for step, n in STEPS:
                if step == "gram" and n[1] == GRAM_PIECES - 1:
                    turn_gram(n[0])
                elif step == "hidden1" and n[1] == H1_PIECES - 1:
                    relu1(n[0])
                elif step == "finish":
                    finish(n)


def kernel(**inputs):
    import numpy as np
    import concourse.bacc as bacc
    from concourse.bass_utils import run_bass_kernel_spmd

    nc = bacc.Bacc("TRN2", target_bir_lowering=False, num_devices=1)
    arrays = {}

    def give(name, a):
        name = "in_" + name
        a = np.ascontiguousarray(a)
        arrays[name] = a
        return nc.dram_tensor(name, a.shape, mybir.dt.from_np(a.dtype), kind="ExternalInput").ap()

    w1 = np.asarray(inputs["W_top1"])
    ids = np.asarray(inputs["ids"])
    n_pairs = CHUNKS * CHUNK
    rownum = np.concatenate([np.arange(TP_ROWS)[:, None] * c + np.arange(MAX_CHUNKS)[None, :] for c in (8, 10)], 1)
    args = [
        give("ids", ids),
        give("ids_small", ids.T[SMALL]),
        give("dense", inputs["r_dense_features"]),
        [give(f"tbl_{t}", inputs[f"tbl_{t}"]) for t in range(N_TABLES)],
        give("w_dense", np.concatenate([w1[0:D], w1[D + n_pairs:]], 0)),
        give("w_pairs", w1[pair_rows()]),
        give("b1", inputs["b_top1"]),
        give("w2", inputs["W_top2"]),
        give("b2", inputs["b_top2"]),
        give("w3", inputs["W_top3"]),
        give("ident", np.eye(P, dtype=np.float32)),
        give("rownum", rownum.astype(np.float32)),
    ]
    out = nc.dram_tensor("out_0", (B, 1), mybir.dt.float32, kind="ExternalOutput").ap()
    dlrm_tower(nc, *args, out)
    return run_bass_kernel_spmd(nc, [arrays], core_ids=[0]).results[0]["out_0"]
```

```python
import concourse.bass as bass
from concourse import mybir
from contextlib import ExitStack

N_TABLES = 26
NF = N_TABLES + 1
B, D = 512, 128
P = 128
TILES = B // P
H1, H2 = 512, 256
ROWS = [12500, 12500, 125000, 12500, 1000, 12500, 1000, 1250, 1250, 12500, 1250, 1000, 12500, 1000, 1250, 1250,
        12500, 1000, 12500, 1250, 1000, 1250, 1250, 1250, 1250, 1000]
SMALL = [4, 6, 11, 13, 17, 20, 25, 7, 8]
GATHERED = [t for t in range(N_TABLES) if t not in SMALL]
TP_ROWS = 125
SPREAD = TP_ROWS // 16 * 16
MAX_CHUNKS = max(ROWS[t] for t in SMALL) // TP_ROWS
ORDER = [0] + [t + 1 for t in GATHERED] + [t + 1 for t in SMALL]
POS_GATHERED, POS_SMALL = 1, 1 + len(GATHERED)
GROUPS = [(t, f, min(f + 4, len(GATHERED))) for t in range(TILES) for f in range(0, len(GATHERED), 4)]
GROUPS_BEFORE = [sum(g[0] < t for g in GROUPS) for t in range(TILES + 1)]

DIAGS = (NF - 1) // 2
PAIRS = DIAGS * NF
CHUNKS = 3
CHUNK = PAIRS // CHUNKS
SQ = 32
SPAN = NF + DIAGS


def pair_rows():
    rows = []
    for d in range(1, DIAGS + 1):
        for f in range(NF):
            i, j = sorted((ORDER[f], ORDER[(f + d) % NF]))
            rows.append(D + i * NF - i * (i + 1) // 2 + (j - i - 1))
    return rows


def dlrm_tower(nc, ids, ids_small, dense, tables, w_dense, w_pairs, b1, w2, b2, w3, ident_src, rownum_src, out):
    fp32, fp32r, i32, u32 = mybir.dt.float32, mybir.dt.float32r, mybir.dt.int32, mybir.dt.uint32
    ALU, ACT = mybir.AluOpType, mybir.ActivationFunctionType
    K = len(SMALL)
    NG = len(GATHERED)
    RAWS, SPLITS, HOTS, ACT_HOTS = 3, 2, 6, 3
    HALVED = 2
    WARM_UPS = 10
    WEIGHT_LOADS = 6

    with ExitStack() as ctx:
        def sb(name, shape, dt=fp32):
            return ctx.enter_context(nc.sbuf_tensor(name, shape, dt))

        def ps(name, shape):
            return ctx.enter_context(nc.psum_tensor(name, shape, fp32))

        def sem(name):
            return ctx.enter_context(nc.semaphore(name))

        idx = sb("idx", [P, TILES, N_TABLES], i32)
        ident = sb("ident", [P, P])
        rownum = sb("rownum", [P, 2 * MAX_CHUNKS])
        ids_rep = sb("ids_rep", [P, RAWS, B], i32)
        raw = sb("raw", [TP_ROWS, RAWS, MAX_CHUNKS * D])
        hi = sb("hi", [TP_ROWS, SPLITS, MAX_CHUNKS * D], fp32r)
        lo = sb("lo", [TP_ROWS, SPLITS, MAX_CHUNKS * D], fp32r)
        hot = sb("hot", [TP_ROWS, HOTS, B], fp32r)
        act_hot = sb("act_hot", [TP_ROWS, ACT_HOTS, B], fp32r)
        distance = sb("distance", [TP_ROWS, B])
        rows = sb("rows", [P, TILES, NG, D])
        dense_sb = sb("dense_sb", [P, TILES, D])
        dense_t = sb("dense_t", [D, B])
        feat = sb("feat", [D, B, NF])
        gram_t = sb("gram_t", [P, SPAN * SQ])
        pairs_s = sb("pairs_s", [P, 2, PAIRS])
        pairs = sb("pairs", [P, 2, CHUNKS, P])
        wd = sb("wd", [P, 2, H1])
        wds = sb("wds", [P, H1])
        wp = sb("wp", [CHUNK + 1, CHUNKS, H1])
        w2_sb = sb("w2_sb", [P, H1 // P, H2])
        b2_sb = sb("b2_sb", [P, H2 // P])
        w3_sb = sb("w3_sb", [P, H2 // P])
        h1 = sb("h1", [P, H1 // P * P])
        h2 = sb("h2", [P, H2 // P * P])
        y = sb("y", [1, B])
        warm = sb("warm", [P, 4 * P], mybir.dt.bfloat16)

        turn_ps = ps("turn_ps", [P, 2, 4 * P])
        gram_a = ps("gram_a", [P, SQ * SQ])
        gram_b = ps("gram_b", [P, SQ * SQ])
        mlp_ps = ps("mlp_ps", [P, 2, 4 * P])
        look_ps = gram_b[:, :].rearrange("p (k b) -> p k b", k=2)
        gram_ps = [gram_a, gram_b]

        idx_in = sem("idx_in")
        const_in = sem("const_in")
        dense_in = sem("dense_in")
        weights_in = sem("weights_in")
        rownum_in = sem("rownum_in")
        ids_in = [sem(f"ids_in{k}") for k in range(RAWS)]
        half_in = sem("half_in")
        table_in = [sem(f"table_in{k}") for k in range(K)]
        rows_in = [sem(f"rows_in{n}") for n in range(len(GROUPS))]
        hi_done = sem("hi_done")
        lo_done = sem("lo_done")
        hot_done = sem("hot_done")
        hot_used = sem("hot_used")
        distance_done = sem("distance_done")
        act_hot_done = sem("act_hot_done")
        act_hot_used = sem("act_hot_used")
        look_out = sem("look_out")
        turn_done = sem("turn_done")
        turn_out = sem("turn_out")
        dense_out = sem("dense_out")
        warm_cleared = sem("warm_cleared")
        gram_cleared = sem("gram_cleared")
        ones_done = sem("ones_done")
        wsum_done = sem("wsum_done")
        gram_done = sem("gram_done")
        gram_half = sem("gram_half")
        gram_out = sem("gram_out")
        picked = sem("picked")
        picked_act = sem("picked_act")
        chunk_out = sem("chunk_out")
        h1_act, h1_dve = sem("h1_act"), sem("h1_dve")
        h2_act, h2_dve = sem("h2_act"), sem("h2_dve")
        h1_done, h1_out = sem("h1_done"), sem("h1_out")
        h2_done, h2_out = sem("h2_done"), sem("h2_out")
        y_done, y_out = sem("y_done"), sem("y_out")
        stored = sem("stored")

        def chunks(k):
            return ROWS[SMALL[k]] // TP_ROWS

        def parts(k):
            w = chunks(k) * D
            return [(0, w // 2), (w // 2, w)] if k < HALVED else [(0, w)]

        PARTS_BEFORE = [sum(len(parts(i)) for i in range(k)) for k in range(K + 1)]

        def row_column(k, c):
            return MAX_CHUNKS + c if chunks(k) == MAX_CHUNKS else c

        def skewed_gram(first, end):
            whole = gram_t[:, :]
            return bass.AP(whole.tensor, whole.offset + SQ + (SQ + 1) * first,
                           [whole.ap[0], [SQ, DIAGS], [SQ + 1, end - first]])

        def picked_pairs(t, first, end):
            return pairs_s[:, t % 2, :].rearrange("p (d f) -> p d f", f=NF)[:, :, first:end]

        ACT_CHUNKS = [2 if chunks(k) == MAX_CHUNKS else 1 for k in range(K)]
        HOTS_BEFORE = [sum(chunks(i) - ACT_CHUNKS[i] for i in range(k)) for k in range(K + 1)]
        ACT_HOTS_BEFORE = [sum(ACT_CHUNKS[:k]) for k in range(K + 1)]

        EARLY = [[], [], [0, 1], [2], [3, 4], [5], [6], [7], [8, 9]]
        GRAM_PIECES = 8
        H1_PIECES = H1 // P
        last_t = TILES - 1
        group = sum(len(e) for e in EARLY)

        def rows_until(end):
            nonlocal group
            steps = [("rows", n) for n in range(group, end)]
            group = max(group, end)
            return steps

        def gram_pieces(t, first, end):
            return [("gram", (t, i)) for i in range(first, end)]

        def hidden1_pieces(t, first, end):
            return [("hidden1", (t, m)) for m in range(first, end)]

        STEPS = gram_pieces(0, 0, 8) + gram_pieces(1, 0, 5) + [("pairs", 0)] + gram_pieces(1, 5, 7)
        STEPS += hidden1_pieces(0, 0, 4) + gram_pieces(1, 7, 8)
        STEPS += rows_until(GROUPS_BEFORE[2] + 2) + [("hidden2", 0), ("pairs", 1)]
        STEPS += rows_until(GROUPS_BEFORE[2] + 3) + [("output", 0)] + rows_until(GROUPS_BEFORE[3])
        STEPS += hidden1_pieces(1, 0, 2) + gram_pieces(2, 0, 4) + hidden1_pieces(1, 2, 4) + gram_pieces(2, 4, 8)
        STEPS += rows_until(GROUPS_BEFORE[3] + 1) + [("hidden2", 1), ("pairs", 2)]
        STEPS += rows_until(GROUPS_BEFORE[3] + 2) + [("output", 1)] + rows_until(GROUPS_BEFORE[3] + 3)
        STEPS += hidden1_pieces(2, 0, 3) + rows_until(GROUPS_BEFORE[4] - 1) + [("dense", last_t)]
        STEPS += rows_until(GROUPS_BEFORE[4]) + hidden1_pieces(2, 3, 4)
        STEPS += gram_pieces(last_t, 0, 8)
        STEPS += [("pick", last_t), ("hidden2", 2), ("pairs", last_t), ("output", 2), ("finish", last_t)]

        JOBS = [("dense", 0)] + [("rows", n) for e in EARLY for n in e]
        JOBS += [step for step in STEPS if step[0] in ("rows", "pairs")]
        JOB = {job: i for i, job in enumerate(JOBS)}
        wide_ps = [mlp_ps[:, 1, 0:P], gram_a[:, 0:P], gram_a[:, 4 * P:5 * P],
                   turn_ps[:, (JOB["pairs", last_t] + 1) % 2, 0:P]]

        block = ctx.enter_context(nc.Block())

        @block.sync
        def _(sp):
            def load_table(k):
                c = chunks(k)
                if k >= RAWS:
                    sp.wait_ge(lo_done, PARTS_BEFORE[k - RAWS + 1])
                    sp.wait_ge(hot_done, HOTS_BEFORE[k - RAWS + 1])
                    sp.wait_ge(distance_done, ACT_HOTS_BEFORE[k - RAWS + 1])
                sp.dma_start(ids_rep[:, k % RAWS, :], ids_small[k:k + 1, :].to_broadcast([P, B])
                             ).then_inc(ids_in[k % RAWS], 16)
                table = tables[SMALL[k]].rearrange("(p c) d -> p (c d)", c=c)
                if k == 0:
                    half = chunks(0) // 2 * D
                    sp.dma_start(raw[0:SPREAD, 0, 0:half], table[0:SPREAD, 0:half]).then_inc(half_in, 16)
                    sp.dma_start(raw[SPREAD:TP_ROWS, 0, 0:c * D], table[SPREAD:TP_ROWS]).then_inc(half_in, 16)
                    sp.dma_start(raw[0:SPREAD, 0, half:c * D], table[0:SPREAD, half:]).then_inc(table_in[0], 16)
                else:
                    sp.dma_start(raw[0:SPREAD, k % RAWS, 0:c * D], table[0:SPREAD]).then_inc(table_in[k], 16)
                    sp.dma_start(raw[SPREAD:TP_ROWS, k % RAWS, 0:c * D],
                                 table[SPREAD:TP_ROWS]).then_inc(table_in[k], 16)

            sp.dma_start(idx[:], ids.rearrange("(t p) f -> p t f", p=P)).then_inc(idx_in, 16)
            sp.dma_start(rownum[:], rownum_src).then_inc(rownum_in, 16)
            load_table(0)
            load_table(1)
            sp.dma_start(ident[:], ident_src).then_inc(const_in, 16)
            load_table(2)
            sp.dma_start(dense_sb[:], dense.rearrange("(t p) d -> p t d", p=P)).then_inc(dense_in, 16)
            for k in range(3, K):
                load_table(k)
            sp.dma_start(wd[:], w_dense.rearrange("(a p) n -> p a n", p=P)).then_inc(weights_in, 16)
            sp.dma_start(wp[0:CHUNK, :, :], w_pairs.rearrange("(c p) n -> p c n", p=CHUNK)).then_inc(weights_in, 16)
            sp.dma_start(wp[CHUNK:CHUNK + 1, 0, :], b1.rearrange("(a n) -> a n", a=1)).then_inc(weights_in, 16)
            sp.dma_start(w2_sb[:], w2.rearrange("(k p) n -> p k n", p=P)).then_inc(weights_in, 16)
            sp.dma_start(b2_sb[:], b2.rearrange("(p k) -> p k", k=H2 // P)).then_inc(weights_in, 16)
            sp.dma_start(w3_sb[:], w3.rearrange("(p k) o -> p (k o)", k=H2 // P)).then_inc(weights_in, 16)
            sp.wait_ge(y_out, TILES)
            sp.dma_start(out.rearrange("b o -> o b"), y[:]).then_inc(stored, 16)
            sp.wait_ge(stored, 16)

        @block.gpsimd
        def _(pool):
            nc.gpsimd.memset(pairs[:], 1.0).then_inc(ones_done, 1)
            pool.wait_ge(idx_in, 16)
            for n, (t, f0, f1) in enumerate(GROUPS):
                for f in range(f0, f1):
                    tab = GATHERED[f]
                    nc.gpsimd.indirect_dma_start(
                        rows[:, t, f, :], None, tables[tab][:, :],
                        bass.IndirectOffsetOnAxis(ap=idx[:, t, tab:tab + 1].bitcast(u32), axis=0),
                    ).then_inc(rows_in[n], 16)

        @block.tensor
        def _(pe):
            def transpose_dense():
                pe.wait_ge(const_in, 16)
                pe.wait_ge(dense_in, 16)
                for t in range(TILES):
                    last = nc.tensor.transpose(turn_ps[:, 0, t * P:(t + 1) * P], dense_sb[:, t, :], ident[:])
                last.then_inc(turn_done, 1)

            def transpose_group(n):
                job = JOB["rows", n]
                t, f0, f1 = GROUPS[n]
                pe.wait_ge(rows_in[n], 16 * (f1 - f0))
                if job >= 2:
                    pe.wait_ge(turn_out, job - 1)
                for f in range(f0, f1):
                    last = nc.tensor.transpose(turn_ps[:, job % 2, (f - f0) * P:(f - f0 + 1) * P],
                                               rows[:, t, f, :], ident[:])
                last.then_inc(turn_done, 1)

            def product(k, c, part, first, last):
                if c < chunks(k) - ACT_CHUNKS[k]:
                    n = HOTS_BEFORE[k] + c
                    pe.wait_ge(hot_done, n + 1)
                    one_hot, used = hot[:, n % HOTS, :], hot_used
                else:
                    n = ACT_HOTS_BEFORE[k] + c - (chunks(k) - ACT_CHUNKS[k])
                    pe.wait_ge(act_hot_done, n + 1)
                    one_hot, used = act_hot[:, n % ACT_HOTS, :], act_hot_used
                done = nc.tensor.matmul(look_ps[:, k % 2, :], part[:, k % SPLITS, c * D:(c + 1) * D],
                                        one_hot, start=first, stop=last)
                if part is lo:
                    done.then_inc(used, 1)

            def look_up(k):
                if k >= 2:
                    pe.wait_ge(look_out, k - 1)
                for i, (w0, w1) in enumerate(parts(k)):
                    cols = range(w0 // D, w1 // D)
                    if (k, i) == (0, 0):
                        pe.wait_ge(hi_done, 1)
                        for c in cols:
                            product(k, c, hi, c == 0, False)
                        pe.wait_ge(lo_done, 1)
                        for c in cols:
                            product(k, c, lo, False, False)
                    else:
                        pe.wait_ge(lo_done, PARTS_BEFORE[k] + i + 1)
                        for c in cols:
                            product(k, c, hi, c == 0, False)
                            product(k, c, lo, False, c == chunks(k) - 1)

            def gram(t, piece):
                if piece == 0:
                    pe.wait_ge(turn_out, JOB["rows", GROUPS_BEFORE[t + 1] - 1] + 1)
                    pe.wait_ge(look_out, K if t == 0 else K + 1)
                    if t == 0:
                        pe.wait_ge(gram_cleared, 1)
                    if t >= 2:
                        pe.wait_ge(gram_out, t - 1)
                for s in range(piece * SQ // GRAM_PIECES, (piece + 1) * SQ // GRAM_PIECES):
                    for j in range(P // SQ):
                        b = t * P + j * SQ + s
                        last = nc.tensor.matmul(gram_ps[t % 2][j * SQ:j * SQ + NF, s * SQ:s * SQ + NF],
                                                feat[:, b, :], feat[:, b, :], start=True, stop=True)
                if piece == GRAM_PIECES - 1:
                    last.then_inc(gram_done, 1)

            def turn_pairs(t):
                job = JOB["pairs", t]
                pe.wait_ge(picked, t + 1)
                if t == last_t:
                    pe.wait_ge(picked_act, 1)
                pe.wait_ge(turn_out, job - 1)
                for c in range(CHUNKS):
                    last = nc.tensor.transpose(turn_ps[0:CHUNK, job % 2, c * P:(c + 1) * P],
                                               pairs_s[:, t % 2, c * CHUNK:(c + 1) * CHUNK], ident[:])
                last.then_inc(turn_done, 1)

            def hidden1(t, m):
                if m == 0:
                    if t == 0:
                        pe.wait_ge(weights_in, 16 * WEIGHT_LOADS)
                        pe.wait_ge(wsum_done, 1)
                        pe.wait_ge(dense_out, 1)
                    if t >= 2:
                        pe.wait_ge(y_out, t - 1)
                    pe.wait_ge(turn_out, JOB["pairs", t] + 1)
                o = mlp_ps[:, t % 2, m * P:(m + 1) * P]
                cols = slice(m * P, (m + 1) * P)
                nc.tensor.matmul(o, wds[:, cols], dense_t[:, t * P:(t + 1) * P], start=True, stop=False)
                for c in range(CHUNKS):
                    k = CHUNK + 1 if c == 0 else CHUNK
                    last = nc.tensor.matmul(o, wp[0:k, c, cols], pairs[0:k, t % 2, c, :],
                                            start=False, stop=(c == CHUNKS - 1))
                if m == H1_PIECES - 1:
                    last.then_inc(h1_done, 1)

            def hidden2(t):
                pe.wait_ge(h1_out, t + 1)
                for m in range(H2 // P):
                    for k in range(H1 // P):
                        w = w2_sb[:, k, :].rearrange("p (q m) -> p m q", m=H2 // P)[:, m, :]
                        last = nc.tensor.matmul(mlp_ps[:, t % 2, m * P:(m + 1) * P], w, h1[:, k * P:(k + 1) * P],
                                                start=(k == 0), stop=(k == H1 // P - 1))
                last.then_inc(h2_done, 1)

            def finish(t):
                for c in range(CHUNKS):
                    pe.wait_ge(chunk_out, c + 1)
                    for m in range(H1_PIECES):
                        k = CHUNK + 1 if c == 0 else CHUNK
                        last = nc.tensor.matmul(wide_ps[m], wp[0:k, c, m * P:(m + 1) * P], pairs[0:k, t % 2, c, :],
                                                start=False, stop=(c == CHUNKS - 1))
                        if c == CHUNKS - 1:
                            last.then_inc(h1_done, 1)
                for k in range(H1_PIECES):
                    if k % 2 == 0:
                        pe.wait_ge(h1_dve, k // 2 + 1)
                    else:
                        pe.wait_ge(h1_act, k // 2 + 1)
                    for m in range(H2 // P):
                        w = w2_sb[:, k, :].rearrange("p (q m) -> p m q", m=H2 // P)[:, m, :]
                        last = nc.tensor.matmul(gram_b[:, m * 4 * P:m * 4 * P + P], w, h1[:, k * P:(k + 1) * P],
                                                start=(k == 0), stop=(k == H1_PIECES - 1))
                        if k == H1_PIECES - 1:
                            last.then_inc(h2_done, 1)
                pe.wait_ge(y_out, t)
                for k in range(H2 // P):
                    if k == 0:
                        pe.wait_ge(h2_act, 1)
                    else:
                        pe.wait_ge(h2_dve, 1)
                    last = nc.tensor.matmul(mlp_ps[0:1, 0, 0:P], w3_sb[:, k:k + 1], h2[:, k * P:(k + 1) * P],
                                            start=(k == 0), stop=(k == H2 // P - 1))
                last.then_inc(y_done, 1)

            def finish_dense(t, first, end):
                if first == 0:
                    pe.wait_ge(y_out, t - 1)
                    pe.wait_ge(gram_out, t)
                else:
                    pe.wait_ge(turn_out, JOB["pairs", t])
                for m in range(first, end):
                    nc.tensor.matmul(wide_ps[m], wds[:, m * P:(m + 1) * P], dense_t[:, t * P:(t + 1) * P],
                                     start=True, stop=False)

            def output(t):
                pe.wait_ge(h2_out, t + 1)
                for k in range(H2 // P):
                    last = nc.tensor.matmul(mlp_ps[0:1, t % 2, 0:P], w3_sb[:, k:k + 1], h2[:, k * P:(k + 1) * P],
                                            start=(k == 0), stop=(k == H2 // P - 1))
                last.then_inc(y_done, 1)

            pe.wait_ge(warm_cleared, 1)
            for i in range(WARM_UPS):
                nc.tensor.matmul(turn_ps[:, 0, :], warm[:, 0:P], warm[:], start=True, stop=True)
            for k in range(K):
                look_up(k)
                if k == 1:
                    transpose_dense()
                for n in EARLY[k]:
                    transpose_group(n)
            for step, n in STEPS:
                if step == "rows":
                    transpose_group(n)
                elif step == "gram":
                    gram(*n)
                elif step == "hidden1":
                    hidden1(*n)
                elif step == "dense":
                    finish_dense(n, 0, H1_PIECES - 1)
                elif step == "pairs":
                    if n == last_t:
                        finish_dense(n, H1_PIECES - 1, H1_PIECES)
                    turn_pairs(n)
                elif step == "hidden2":
                    hidden2(n)
                elif step == "output":
                    output(n)
                elif step == "finish":
                    finish(n)

        @block.scalar
        def _(act):
            def copy_dense():
                act.wait_ge(turn_done, 1)
                nc.scalar.copy(dense_t[:], turn_ps[:, 0, :]).then_inc(dense_out, 1)
                nc.scalar.copy(feat[:, :, 0], turn_ps[:, 0, :]).then_inc(turn_out, 1)

            def copy_group(n):
                job = JOB["rows", n]
                t, f0, f1 = GROUPS[n]
                act.wait_ge(turn_done, job + 1)
                nc.scalar.copy(feat[:, t * P:(t + 1) * P, POS_GATHERED + f0:POS_GATHERED + f1],
                               turn_ps[:, job % 2, 0:(f1 - f0) * P].rearrange("p (f b) -> p b f", f=f1 - f0),
                               ).then_inc(turn_out, 1)

            def split_high(k):
                if k >= SPLITS:
                    act.wait_ge(act_hot_used, ACT_HOTS_BEFORE[k - SPLITS + 1])
                for i, (w0, w1) in enumerate(parts(k)):
                    if (k, i) == (0, 0):
                        act.wait_ge(half_in, 32)
                    else:
                        act.wait_ge(table_in[k], 16 if k == 0 else 32)
                    nc.scalar.copy(hi[:, k % SPLITS, w0:w1], raw[:, k % RAWS, w0:w1]).then_inc(hi_done, 1)

            def act_one_hots(k):
                if k == 0:
                    act.wait_ge(rownum_in, 16)
                act.wait_ge(ids_in[k % RAWS], 16 * (k // RAWS + 1))
                for i in range(ACT_CHUNKS[k]):
                    n = ACT_HOTS_BEFORE[k] + i
                    col = row_column(k, chunks(k) - ACT_CHUNKS[k] + i)
                    if n >= 1:
                        act.wait_ge(act_hot_done, n)
                    nc.scalar.activation(distance[:, :], ids_rep[0:TP_ROWS, k % RAWS, :], ACT.Abs, scale=-1.0,
                                         bias=rownum[0:TP_ROWS, col:col + 1]).then_inc(distance_done, 1)
                    act.wait_ge(distance_done, n + 1)
                    if n >= ACT_HOTS:
                        act.wait_ge(act_hot_used, n - ACT_HOTS + 1)
                    nc.scalar.activation(act_hot[:, n % ACT_HOTS, :], distance[:, :], ACT.Relu, scale=-1.0,
                                         bias=1.0).then_inc(act_hot_done, 1)

            def copy_lookups(k):
                act.wait_ge(act_hot_used, ACT_HOTS_BEFORE[k + 1])
                for b0, b1 in [(0, P), (P, B)] if k == K - 1 else [(0, B)]:
                    nc.scalar.copy(feat[:, b0:b1, POS_SMALL + k], look_ps[:, k % 2, b0:b1]).then_inc(look_out, 1)

            def copy_pairs(t):
                job = JOB["pairs", t]
                act.wait_ge(turn_done, job + 1)
                if t == 0:
                    act.wait_ge(ones_done, 1)
                if t >= 2:
                    act.wait_ge(h1_done, t - 1)
                if t == last_t:
                    for c in range(CHUNKS):
                        nc.scalar.copy(pairs[0:CHUNK, t % 2, c, :],
                                       turn_ps[0:CHUNK, job % 2, c * P:(c + 1) * P]).then_inc(chunk_out, 1)
                    return
                nc.scalar.copy(pairs[0:CHUNK, t % 2, :, :],
                               turn_ps[0:CHUNK, job % 2, 0:CHUNKS * P].rearrange("p (c b) -> p c b", c=CHUNKS),
                               ).then_inc(turn_out, 1)

            def relu2(t):
                act.wait_ge(h2_done, t + 1)
                if t >= 1:
                    act.wait_ge(y_done, t)
                for m in range(H2 // P):
                    last = nc.scalar.activation(h2[:, m * P:(m + 1) * P], mlp_ps[:, t % 2, m * P:(m + 1) * P],
                                                ACT.Relu, bias=b2_sb[:, m:m + 1])
                last.then_inc(h2_out, 1)

            def pick_first(t):
                act.wait_ge(gram_half, t + 1)
                act.wait_ge(turn_done, JOB["pairs", t - 2] + 1)
                nc.scalar.copy(picked_pairs(t, 0, NF - DIAGS), skewed_gram(0, NF - DIAGS)).then_inc(picked_act, 1)

            def finish(t):
                act.wait_ge(h2_done, t)
                for m in (1, 3):
                    act.wait_ge(h1_done, t + m + 1)
                    nc.scalar.activation(h1[:, m * P:(m + 1) * P], wide_ps[m], ACT.Relu).then_inc(h1_act, 1)
                act.wait_ge(y_done, t)
                act.wait_ge(h2_done, t + 1)
                nc.scalar.activation(h2[:, 0:P], gram_b[:, 0:P], ACT.Relu, bias=b2_sb[:, 0:1]).then_inc(h2_act, 1)
                act.wait_ge(y_done, t + 1)
                nc.scalar.copy(y[0:1, t * P:(t + 1) * P], mlp_ps[0:1, 0, 0:P]).then_inc(y_out, 1)

            def copy_output(t):
                act.wait_ge(y_done, t + 1)
                nc.scalar.copy(y[0:1, t * P:(t + 1) * P], mlp_ps[0:1, t % 2, 0:P]).then_inc(y_out, 1)

            split_high(0)
            act_one_hots(0)
            for k in range(K):
                if k + 1 < K:
                    split_high(k + 1)
                    act_one_hots(k + 1)
                copy_lookups(k)
                if k == 1:
                    copy_dense()
                for n in EARLY[k]:
                    copy_group(n)
            act.wait_ge(weights_in, 16 * WEIGHT_LOADS)
            for step, n in STEPS:
                if step == "rows":
                    copy_group(n)
                elif step == "pick":
                    pick_first(n)
                elif step == "pairs":
                    copy_pairs(n)
                elif step == "hidden2":
                    relu2(n)
                elif step == "output":
                    copy_output(n)
                elif step == "finish":
                    finish(n)

        @block.vector
        def _(dve):
            def split_low(k):
                for i, (w0, w1) in enumerate(parts(k)):
                    dve.wait_ge(hi_done, PARTS_BEFORE[k] + i + 1)
                    nc.vector.tensor_tensor(lo[:, k % SPLITS, w0:w1], raw[:, k % RAWS, w0:w1],
                                            hi[:, k % SPLITS, w0:w1].bitcast(fp32),
                                            ALU.subtract).then_inc(lo_done, 1)

            def one_hots(k, c0, c1):
                if k == 0:
                    dve.wait_ge(rownum_in, 16)
                dve.wait_ge(ids_in[k % RAWS], 16 * (k // RAWS + 1))
                for c in range(c0, c1):
                    n = HOTS_BEFORE[k] + c
                    if n >= HOTS:
                        dve.wait_ge(hot_used, n - HOTS + 1)
                    col = row_column(k, c)
                    nc.vector.tensor_scalar(hot[:, n % HOTS, :], ids_rep[0:TP_ROWS, k % RAWS, :],
                                            rownum[0:TP_ROWS, col:col + 1], None, ALU.is_equal).then_inc(hot_done, 1)

            def turn_gram(t):
                dve.wait_ge(gram_done, t + 1)
                if t >= 1:
                    dve.wait_ge(picked, t)
                src = gram_ps[t % 2][:, :].rearrange("p (s g) -> p g s", g=SQ)
                dst = gram_t[:, :].rearrange("p (g f) -> p g f", f=SQ)
                nc.vector.transpose(dst[:, 0:NF, :], src[:, 0:NF, :]).then_inc(gram_half, 1)
                nc.vector.transpose(dst[:, NF:SPAN, :], src[:, 0:DIAGS, :]).then_inc(gram_out, 1)
                dve.wait_ge(gram_out, t + 1)
                if t >= 2:
                    dve.wait_ge(turn_done, JOB["pairs", t - 2] + 1)
                first = NF - DIAGS if t == last_t else 0
                nc.vector.tensor_copy(picked_pairs(t, first, NF), skewed_gram(first, NF)).then_inc(picked, 1)

            def relu1(t):
                dve.wait_ge(h1_done, t + 1)
                if t >= 1:
                    dve.wait_ge(h2_done, t)
                nc.vector.tensor_scalar(h1[:], mlp_ps[:, t % 2, :], 0.0, None, ALU.max).then_inc(h1_out, 1)

            def finish(t):
                dve.wait_ge(h2_done, t)
                for m in (0, 2):
                    dve.wait_ge(h1_done, t + m + 1)
                    nc.vector.tensor_scalar(h1[:, m * P:(m + 1) * P], wide_ps[m], 0.0, None,
                                            ALU.max).then_inc(h1_dve, 1)
                dve.wait_ge(y_done, t)
                dve.wait_ge(h2_done, t + 2)
                nc.vector.tensor_scalar(h2[:, P:2 * P], gram_b[:, 4 * P:5 * P], b2_sb[:, 1:2], 0.0,
                                        ALU.add, ALU.max).then_inc(h2_dve, 1)

            nc.vector.memset(warm[:].bitcast(u32), 0).then_inc(warm_cleared, 1)
            nc.vector.memset(gram_a[:], 0.0).then_inc(gram_cleared, 1)
            one_hots(0, 0, chunks(0) // 2)
            split_low(0)
            one_hots(0, chunks(0) // 2, chunks(0) - ACT_CHUNKS[0])
            for k in range(1, K):
                split_low(k)
                one_hots(k, 0, chunks(k) - ACT_CHUNKS[k])
            dve.wait_ge(weights_in, 16 * WEIGHT_LOADS)
            nc.vector.tensor_tensor(wds[:], wd[:, 0, :], wd[:, 1, :], ALU.add).then_inc(wsum_done, 1)
            for step, n in STEPS:
                if step == "gram" and n[1] == GRAM_PIECES - 1:
                    turn_gram(n[0])
                elif step == "hidden1" and n[1] == H1_PIECES - 1:
                    relu1(n[0])
                elif step == "finish":
                    finish(n)


def kernel(**inputs):
    import numpy as np
    import concourse.bacc as bacc
    from concourse.bass_utils import run_bass_kernel_spmd

    nc = bacc.Bacc("TRN2", target_bir_lowering=False, num_devices=1)
    arrays = {}

    def give(name, a):
        name = "in_" + name
        a = np.ascontiguousarray(a)
        arrays[name] = a
        return nc.dram_tensor(name, a.shape, mybir.dt.from_np(a.dtype), kind="ExternalInput").ap()

    w1 = np.asarray(inputs["W_top1"])
    ids = np.asarray(inputs["ids"])
    n_pairs = CHUNKS * CHUNK
    rownum = np.concatenate([np.arange(P)[:, None] * c + np.arange(MAX_CHUNKS)[None, :] for c in (8, 10)], 1)
    args = [
        give("ids", ids),
        give("ids_small", ids.T[SMALL]),
        give("dense", inputs["r_dense_features"]),
        [give(f"tbl_{t}", inputs[f"tbl_{t}"]) for t in range(N_TABLES)],
        give("w_dense", np.concatenate([w1[0:D], w1[D + n_pairs:]], 0)),
        give("w_pairs", w1[pair_rows()]),
        give("b1", inputs["b_top1"]),
        give("w2", inputs["W_top2"]),
        give("b2", inputs["b_top2"]),
        give("w3", inputs["W_top3"]),
        give("ident", np.eye(P, dtype=np.float32)),
        give("rownum", rownum.astype(np.float32)),
    ]
    out = nc.dram_tensor("out_0", (B, 1), mybir.dt.float32, kind="ExternalOutput").ap()
    dlrm_tower(nc, *args, out)
    return run_bass_kernel_spmd(nc, [arrays], core_ids=[0]).results[0]["out_0"]
```
